# Optimizing a Trainium2 kernel written in Bass

```python
import numpy as np
import jax
import jax.numpy as jnp

def _softmax(x, axis=-1):
    return jax.nn.softmax(x, axis=axis)

def _gelu(x):
    return jax.nn.gelu(x, approximate=True)

def _silu(x):
    return jax.nn.silu(x)

def _sigmoid(x):
    return jax.nn.sigmoid(x)

def _layernorm(x, axis=-1, eps=1e-05):
    m = jnp.mean(x, axis=axis, keepdims=True)
    v = jnp.var(x, axis=axis, keepdims=True)
    return (x - m) / jnp.sqrt(v + eps)

def _scatter_add(tgt, idx, src, axis=0):
    return tgt.at[idx].add(src)

def _segment_sum(src, seg, n):
    return jax.ops.segment_sum(src, seg, n)
kernel_name = 'mk_rec_standalone_d1_rec_r8_120f6f'

def setup_inputs(seed: int=0):
    np.random.seed(seed)
    _w = jnp.asarray

    def _rec_inputs():
        import jax
        import jax.numpy as jnp
        _rk = jax.random.key(seed)
        r_x = -0.000611745 + 1.00059 * jax.random.normal(jax.random.fold_in(_rk, 1), (2048, 39, 16), jnp.float32)
        return r_x
    r_x = _rec_inputs()

    def _L0_rec_setup():
        import jax, jax.numpy as jnp
        import numpy as np
        key = jax.random.key(seed)
        k1, k2, k3 = jax.random.split(key, 3)
        B, M, D = (512, 39, 16)
        H = [128, 128]
        x = jax.random.normal(k1, (B, M, D), dtype=jnp.float32)
        W0 = jax.random.normal(k2, (1, M * M, H[0]), dtype=jnp.float32) * 0.05
        W1 = jax.random.normal(k3, (1, M * H[0], H[1]), dtype=jnp.float32) * 0.05
        return {'x': x, 'W0': W0, 'W1': W1}
    _L0_rec_all = _L0_rec_setup()
    _L0_rec_in = {k: v for k, v in _L0_rec_all.items() if k in ('W0', 'W1')}
    del _L0_rec_all
    return {'r_x': r_x, 'L0_rec_W0': _L0_rec_in['W0'], 'L0_rec_W1': _L0_rec_in['W1']}

def reference(r_x, L0_rec_W0, L0_rec_W1):
    import jax
    import jax.numpy as jnp

    def _L0_rec_ref(x, W0, W1):
        import jax, jax.numpy as jnp
        import numpy as np
        m = x.shape[1]
        x0 = x
        xk = x
        outs = []
        for W in (W0, W1):
            Hk = xk.shape[1]
            Hn = W.shape[-1]
            Wr = W.reshape(m, Hk, Hn)
            xk = jnp.einsum('bid,bjd,ijh->bhd', x0, xk, Wr)
            outs.append(xk)
        result = jnp.concatenate(outs, axis=1)
        return jnp.sum(result, axis=-1)
    y = _L0_rec_ref(r_x, L0_rec_W0, L0_rec_W1)
    return y

_drawn_inputs = setup_inputs


def setup_inputs(seed=0):
    import zlib

    import numpy as np

    out = dict(_drawn_inputs(seed))
    spreads = {}
    factors = {}
    for name, (base, spread) in spreads.items():
        noise = np.random.default_rng([zlib.crc32(name.encode()), seed]).standard_normal(out[name].shape)
        drawn = base * np.exp(spread * noise) if base else spread * noise
        out[name] = jnp.asarray(drawn.astype(out[name].dtype))
    for name, factor in factors.items():
        out[name] = (out[name] * factor).astype(out[name].dtype)
    return out
```

```python
from contextlib import ExitStack

import numpy as np

import concourse.bass as bass
from concourse import mybir

F32 = mybir.dt.float32
F32R = mybir.dt.float32r
ALU = mybir.AluOpType
COPY = mybir.ActivationFunctionType.Copy

P = 128
B, M, D = 2048, 39, 16
H = 128
GC = 1024
HC = GC // 2
NG = B * D // GC
TILES = 7
FULL = TILES - 1
LEFT = range(18, 30)
LEFT_HI, LEFT_HI2, LEFT_LO = 0, M, 2 * M
NQ = GC // P
BQ = P // D
MI = M + 1
CB = 4
NB = CB * GC // D
NCH = NG // CB
LO_ROW = 64
LO_AT = 2 * M
POOL_LO = (1, 3, 5)
DVE_LO = (0, 2, 4, 6)
NW = 4
PIECES = -(-M // NW)
FILLS = [("rep", 0), ("rep", 1), ("turn", 0)] + [("rep", t) for t in range(2, TILES)]
STEPS = len(FILLS)
POS = {f: k for k, f in enumerate(FILLS)}


def pair_slots():
    left = set(LEFT)
    cap = [FULL * len(range(v, P, M)) for v in range(M)]
    own = {(i, i): i for i in range(M) if i not in left}
    for i in range(M):
        for s in range(1, (M + 1) // 2):
            j = (i + s) % M
            own[min(i, j), max(i, j)] = i
    count = [0] * M
    for v in own.values():
        count[v] += 1
    for v in range(M):
        while count[v] < cap[v]:
            back, queue, found = {v: None}, [v], None
            while queue and found is None:
                a = queue.pop(0)
                for u in range(M):
                    if u not in back and own[min(u, a), max(u, a)] == u:
                        back[u] = a
                        queue.append(u)
                        if count[u] > cap[u]:
                            found = u
                            break
            u = found
            while back[u] is not None:
                a = back[u]
                own[min(u, a), max(u, a)] = a
                u = a
            count[found] -= 1
            count[v] += 1
    assert count == cap
    free = {v: [(t, m) for t in range(FULL) for m in range(v, P, M)] for v in range(M)}
    slots = [(*free[v].pop(), v, i + j - v) for (i, j), v in sorted(own.items())]
    for i in LEFT:
        slots += [(FULL, r + i, i, i) for r in (LEFT_HI, LEFT_HI2, LEFT_LO)]
    return slots


def build(nc, xa, xd, w0a, w0b, w1, sel, ident, out):
    with ExitStack() as ctx:
        def sb(name, shape, dt=F32):
            return ctx.enter_context(nc.sbuf_tensor(name, shape, dt))

        def sem(name):
            return ctx.enter_context(nc.semaphore(name))

        w0h = sb("w0h", [P, TILES, H], F32R)
        w0l = sb("w0l", [P, TILES, H], F32R)
        selr = sb("selr", [P, TILES, P], F32R)
        w1h = sb("w1h", [P, M, H], F32R)
        w1l = sb("w1l", [P, M, H], F32R)
        gh = sb("gh", [P, MI, NB], F32R)
        gl = sb("gl", [P, MI, NB], F32R)
        xs = sb("xs", [P, 2, GC])
        xhl = sb("xhl", [P, 2, GC], F32R)
        f = sb("f", [P, 2, GC])
        fh = sb("fh", [P, 2, GC], F32R)
        fl = sb("fl", [P, 2, GC], F32R)
        x1 = sb("x1", [P, GC])
        x1th = sb("x1th", [P, NQ, H], F32R)
        x1tl = sb("x1tl", [P, NQ, H], F32R)
        xdr = sb("xdr", [P, NQ, MI])
        xdhl = sb("xdhl", [P, NQ, 2, MI], F32R)
        xbd = sb("xbd", [P, NQ, 2, BQ, MI], F32R)
        outs = sb("outs", [P, 2, NB])
        idn = sb("idn", [P, P])
        ring = ctx.enter_context(nc.psum_tensor("ring", [P, 2, GC], F32))
        acc = ctx.enter_context(nc.psum_tensor("acc", [P, 2, HC], F32))
        pg = ctx.enter_context(nc.psum_tensor("pg", [P, 2, HC], F32))

        consts_in = sem("consts_in")
        ident_in = sem("ident_in")
        sel_ready = sem("sel_ready")
        w0_sum = sem("w0_sum")
        w0_high = sem("w0_high")
        w0_ready = sem("w0_ready")
        xbd_zero = sem("xbd_zero")
        w1_in = sem("w1_in")
        w1_high = sem("w1_high")
        w1_ready = sem("w1_ready")
        xs_in = [sem("xs_in0"), sem("xs_in1")]
        x_high = sem("x_high")
        x_low = sem("x_low")
        xd_in = sem("xd_in")
        xd_high = sem("xd_high")
        xd_low = sem("xd_low")
        xbd_in = sem("xbd_in")
        rep_done = sem("rep_done")
        prod_done = sem("prod_done")
        high_done = sem("high_done")
        low_dve = sem("low_dve")
        low_pool = sem("low_pool")
        main_done = sem("main_done")
        acc_done = sem("acc_done")
        x1_a = sem("x1_a")
        x1_b = sem("x1_b")
        turned = sem("turned")
        x1t_high = sem("x1t_high")
        x1t_low = sem("x1t_low")
        g_done = sem("g_done")
        g_high = sem("g_high")
        g_low = sem("g_low")
        fin_done = sem("fin_done")
        out1_ready = sem("out1_ready")
        out2_ready = sem("out2_ready")
        outs_dma = sem("outs_dma")

        def tile_n(g, t):
            return TILES * g + t + 1

        def wait_low(eng, g, t):
            if t in POOL_LO:
                eng.wait_ge(low_pool, len(POOL_LO) * g + POOL_LO.index(t) + 1)
            else:
                eng.wait_ge(low_dve, len(DVE_LO) * g + DVE_LO.index(t) + 1)

        def buf(gi, t):
            return (TILES * gi + t) % 2

        def before(gi, t, back):
            n = t - back
            return (0, n) if n >= 0 else (-1, n + TILES)

        def g_at(gi, q):
            b0 = ((gi - 1) % CB) * (NB // CB) + q * BQ
            return slice(b0, b0 + BQ)

        def g_psum(q):
            return pg[:, q % 2, 0:BQ * MI].rearrange("p (b i) -> p i b", b=BQ)

        block = ctx.enter_context(nc.Block())

        @block.sync
        def _(sp):
            sp.dma_start(xs[:, 0, :], xa[0]).then_inc(xs_in[0], 16)
            sp.dma_start(f[:, 0, 0:TILES * P], sel).then_inc(consts_in, 16)
            sp.dma_start(f[:, 1, 0:TILES * H], w0a).then_inc(consts_in, 16)
            sp.dma_start(x1[:, 0:TILES * H], w0b).then_inc(consts_in, 16)
            sp.dma_start(xdr[:, :, :], xd[0]).then_inc(xd_in, 16)
            sp.dma_start(idn[:, :], ident).then_inc(ident_in, 16)

            def w1_load(p):
                n = min(NW, M - NW * p)
                if p:
                    sp.wait_ge(w1_ready, p)
                sp.dma_start(outs[:, :, :].rearrange("p a b -> p (a b)")[:, 0:n * H],
                             w1[:, NW * p * H:(NW * p + n) * H])\
                  .then_inc(w1_in if p < PIECES - 1 else outs_dma, 16)

            def blocks(g, first):
                if first:
                    sp.wait_ge(xbd_zero, 1)
                else:
                    sp.wait_ge(g_done, NQ * g)
                sp.wait_ge(xd_low, g + 1)
                for b in range(BQ):
                    sp.dma_start(xbd[D * b:D * b + D, :, :, b, :].rearrange("p q s i -> p (q s) i").bitcast(F32),
                                 xdhl[D * b:D * b + D, :, :, :].rearrange("p q s i -> p (q s) i").bitcast(F32))\
                      .then_inc(xbd_in, 16)

            def send(c, out_at):
                sp.wait_ge(out1_ready, c + 1)
                sp.wait_ge(out2_ready, c + 1)
                sp.dma_start(out_at, outs[:, :, :]).then_inc(outs_dma, 16)

            def chunk(j, first, last):
                for gi in range(CB):
                    g = CB * j + gi
                    if not (last and gi == CB - 1):
                        if not (first and gi == 0):
                            sp.wait_ge(prod_done, TILES * g)
                            sp.wait_ge(x_low, g)
                        sp.dma_start(xs[:, (gi + 1) % 2, :], xa[g + 1]).then_inc(xs_in[(gi + 1) % 2], 16)
                    if not (first and gi == 0):
                        blocks(g - 1, first and gi == 1)
                    if not (last and gi == CB - 1):
                        sp.wait_ge(xd_low, g + 1)
                        sp.dma_start(xdr[:, :, :], xd[g + 1]).then_inc(xd_in, 16)
                    if gi == 2 and not first:
                        send(j - 1, out[j - 1])
                    if first:
                        for p in range(3 * gi + 1, min(3 * gi + 4, PIECES)):
                            w1_load(p)

            w1_load(0)
            chunk(0, True, False)
            with sp.Fori(1, NCH - 1) as j:
                chunk(j, False, False)
            chunk(NCH - 1, False, True)
            blocks(NG - 1, False)
            send(NCH - 1, out[NCH - 1])
            sp.wait_ge(outs_dma, 16 * (NCH + 1))

        @block.tensor
        def _(pe):
            def fill_rep(g, gi, t, slot, first):
                if t == 0:
                    pe.wait_ge(x_high, g + 1)
                    pe.wait_ge(x_low, g + 1)
                for half in range(2):
                    last = nc.tensor.matmul(ring[:, slot, half * HC:(half + 1) * HC], selr[:, t, :],
                                            xhl[:, gi % 2, half * HC:(half + 1) * HC], start=True, stop=True)
                last.then_inc(rep_done, 1)

            def fill_turn(g, slot):
                pe.wait_ge(x1_a, g + 1)
                pe.wait_ge(x1_b, g + 1)
                for q in range(NQ):
                    last = nc.tensor.transpose(ring[:, slot, q * H:(q + 1) * H], x1[:, q * P:(q + 1) * P],
                                               idn[:, :])
                last.then_inc(turned, 1)

            def fill(g, gi, k, first):
                kind, t = FILLS[k]
                if first and gi == 0 and k == POS["turn", 0]:
                    return
                was = k - 2
                if was < 0:
                    if not (first and gi == 0):
                        pe.wait_ge(prod_done, tile_n(g - 1, FILLS[was + STEPS][1]))
                elif FILLS[was][0] == "turn":
                    if first and gi == 0:
                        pe.wait_ge(prod_done, tile_n(g, 0))
                    else:
                        pe.wait_ge(x1t_high, g)
                        pe.wait_ge(x1t_low, g)
                else:
                    pe.wait_ge(prod_done, tile_n(g, FILLS[was][1]))
                if kind == "rep":
                    fill_rep(g, gi, t, k % 2, first)
                else:
                    fill_turn(g - 1, k % 2)

            def main(g, gi, t):
                pe.wait_ge(high_done, tile_n(g, t))
                wait_low(pe, g, t)
                s = buf(gi, t)
                for half in range(2):
                    c = slice(half * HC, (half + 1) * HC)
                    if t < FULL:
                        nc.tensor.matmul(acc[:, half, :], w0h[:, t, :], fh[:, s, c], start=t == 0, stop=False)
                        nc.tensor.matmul(acc[:, half, :], w0l[:, t, :], fh[:, s, c], start=False, stop=False)
                        last = nc.tensor.matmul(acc[:, half, :], w0h[:, t, :], fl[:, s, c],
                                                start=False, stop=False)
                    else:
                        last = nc.tensor.matmul(acc[:, half, :], w0l[:, t, :], fh[:, s, c],
                                                start=False, stop=True).then_inc(acc_done, 1)
                if t < FULL:
                    last.then_inc(main_done, 1)

            def g_tile(g, q, fresh, after_final):
                if q == 0:
                    pe.wait_ge(x1t_high, g + 1)
                    pe.wait_ge(x1t_low, g + 1)
                    pe.wait_ge(xbd_in, 16 * BQ * (g + 1))
                    if after_final is not None:
                        pe.wait_ge(out2_ready, after_final)
                if not (fresh and q < 2):
                    pe.wait_ge(g_low, NQ * g + q - 1)
                o = pg[:, q % 2, 0:BQ * MI]
                xh = xbd[:, q, 0, :, :].rearrange("p b i -> p (b i)")
                xl = xbd[:, q, 1, :, :].rearrange("p b i -> p (b i)")
                nc.tensor.matmul(o, x1th[:, q, :], xh, start=True, stop=False)
                nc.tensor.matmul(o, x1th[:, q, :], xl, start=False, stop=False)
                nc.tensor.matmul(o, x1tl[:, q, :], xh, start=False, stop=True).then_inc(g_done, 1)

            def final(c):
                pe.wait_ge(g_high, CB * NQ * (c + 1))
                pe.wait_ge(g_low, CB * NQ * (c + 1))
                pe.wait_ge(w1_ready, PIECES)
                o = pg[:, 0, 0:NB]
                for i in range(M):
                    nc.tensor.matmul(o, w1h[:, i, :], gh[:, i, :], start=i == 0, stop=False)
                    nc.tensor.matmul(o, w1l[:, i, :], gh[:, i, :], start=False, stop=False)
                    last = nc.tensor.matmul(o, w1h[:, i, :], gl[:, i, :], start=False, stop=i == M - 1)
                last.then_inc(fin_done, 1)

            def chunk(j, first, last):
                for gi in range(CB):
                    g = CB * j + gi
                    for k in range(STEPS):
                        if k + 2 < STEPS:
                            fill(g, gi, k + 2, first)
                        elif not (last and gi == CB - 1):
                            fill(g + 1, (gi + 1) % CB, k + 2 - STEPS, False)
                        kind, t = FILLS[k]
                        if kind == "rep":
                            main(g, gi, t)
                        if k >= STEPS // 2 and not (first and gi == 0):
                            for q in (2 * k - STEPS, 2 * k - STEPS + 1):
                                g_tile(g - 1, q, first and gi == 1, j if gi == 1 and not first else None)
                        if k == 0 and gi == 1 and not first:
                            final(j - 1)

            pe.wait_ge(sel_ready, 1)
            fill(0, 0, 0, True)
            fill(0, 0, 1, True)
            pe.wait_ge(w0_ready, 2)
            pe.wait_ge(ident_in, 16)
            chunk(0, True, False)
            with pe.Fori(1, NCH - 1) as j:
                chunk(j, False, False)
            chunk(NCH - 1, False, True)
            fill_turn(NG - 1, 0)
            for q in range(NQ):
                g_tile(NG - 1, q, False, None)
            final(NCH - 1)

        @block.scalar
        def _(act):
            def high(g, gi, t, first):
                act.wait_ge(prod_done, tile_n(g, t))
                if not (first and gi == 0 and t < 2):
                    dg, dt = before(gi, t, 2)
                    wait_main(act, g + dg, dt)
                nc.scalar.activation(fh[:, buf(gi, t), :], f[:, buf(gi, t), :], COPY).then_inc(high_done, 1)

            def x1_first_half(g):
                act.wait_ge(acc_done, 2 * g + 1)
                nc.scalar.activation(x1[:, 0:HC], acc[:, 0, :], COPY).then_inc(x1_a, 1)

            def xd_split(g, first):
                act.wait_ge(xd_in, 16 * (g + 1))
                if not first:
                    act.wait_ge(xbd_in, 16 * BQ * g)
                nc.scalar.activation(xdhl[:, :, 0, :], xdr[:, :, :], COPY).then_inc(xd_high, 1)

            def turned_high(g):
                act.wait_ge(turned, g + 1)
                nc.scalar.activation(x1th[:, :, :], ring[:, 0, :].rearrange("p (q h) -> p q h", h=H), COPY)\
                  .then_inc(x1t_high, 1)

            def g_highs(g, gi, qs, freed):
                for q in qs:
                    act.wait_ge(g_done, NQ * g + q + 1)
                    if q == 0 and freed is not None:
                        act.wait_ge(fin_done, freed)
                        act.wait_ge(out1_ready, freed)
                    nc.scalar.activation(gh[:, :, g_at(gi, q)], g_psum(q), COPY).then_inc(g_high, 1)

            def final_out(c):
                act.wait_ge(fin_done, c + 1)
                act.wait_ge(outs_dma, 16 * (c + 1))
                nc.scalar.activation(outs[:, 1, :], pg[:, 0, 0:NB], COPY).then_inc(out2_ready, 1)

            def w1_piece(p):
                n = min(NW, M - NW * p)
                if p < PIECES - 1:
                    act.wait_ge(w1_in, 16 * (p + 1))
                else:
                    act.wait_ge(outs_dma, 16)
                nc.scalar.activation(w1h[:, NW * p:NW * p + n, :],
                                     outs[:, :, :].rearrange("p a b -> p (a b)")[:, 0:n * H], COPY)\
                  .then_inc(w1_high, 1)

            def wait_main(eng, g, t):
                if t == FULL:
                    eng.wait_ge(acc_done, 2 * g + 2)
                else:
                    eng.wait_ge(main_done, FULL * g + t + 1)

            def chunk(j, first, last):
                for gi in range(CB):
                    g = CB * j + gi
                    prev = not (first and gi == 0)
                    final_group = last and gi == CB - 1
                    piece = 3 * gi if first else PIECES
                    high(g, gi, 0, first)
                    if prev:
                        x1_first_half(g - 1)
                    if prev and not (first and gi == 1):
                        g_highs(g - 2, gi - 1, (6, 7), None)
                    if gi == 1 and not first:
                        final_out(j - 1)
                    high(g, gi, 1, first)
                    if not final_group:
                        act.wait_ge(xs_in[(gi + 1) % 2], 32 * j + 16 * ((gi + 1) // 2 + 1))
                        if prev:
                            act.wait_ge(rep_done, TILES * g)
                        nc.scalar.activation(xhl[:, (gi + 1) % 2, :], xs[:, (gi + 1) % 2, :], COPY)\
                          .then_inc(x_high, 1)
                    if prev:
                        turned_high(g - 1)
                    high(g, gi, 2, first)
                    xd_split(g, not prev)
                    if piece < PIECES:
                        w1_piece(piece)
                    high(g, gi, 3, first)
                    high(g, gi, 4, first)
                    if prev:
                        g_highs(g - 1, gi, (0, 1), (j if not first else None) if gi == 1 else None)
                    if piece + 1 < PIECES:
                        w1_piece(piece + 1)
                    high(g, gi, 5, first)
                    if prev:
                        g_highs(g - 1, gi, (2, 3), None)
                    if piece + 2 < PIECES:
                        w1_piece(piece + 2)
                    high(g, gi, 6, first)
                    if prev:
                        g_highs(g - 1, gi, (4, 5), None)

            act.wait_ge(xs_in[0], 16)
            nc.scalar.activation(xhl[:, 0, :], xs[:, 0, :], COPY).then_inc(x_high, 1)
            act.wait_ge(consts_in, 48)
            nc.scalar.activation(selr[:, :, :], f[:, 0, 0:TILES * P].rearrange("p (t m) -> p t m", m=P), COPY)\
              .then_inc(sel_ready, 1)
            act.wait_ge(w0_sum, 1)
            nc.scalar.activation(w0h[:, :, :], f[:, 1, 0:TILES * H].rearrange("p (t h) -> p t h", h=H), COPY)\
              .then_inc(w0_high, 1)
            nc.scalar.activation(w0l[:, FULL, :], x1[:, FULL * H:TILES * H], COPY).then_inc(w0_high, 1)
            chunk(0, True, False)
            with act.Fori(1, NCH - 1) as j:
                chunk(j, False, False)
            chunk(NCH - 1, False, True)
            x1_first_half(NG - 1)
            g_highs(NG - 2, CB - 1, (6, 7), None)
            turned_high(NG - 1)
            g_highs(NG - 1, CB, range(NQ), None)
            final_out(NCH - 1)

        @block.vector
        def _(dve):
            def product(g, gi, t, first):
                s = buf(gi, t)
                dve.wait_ge(rep_done, tile_n(g, t))
                if not (first and gi == 0 and t < 2):
                    dg, dt = before(gi, t, 2)
                    dve.wait_ge(high_done, tile_n(g + dg, dt))
                    wait_low(dve, g + dg, dt)
                nc.vector.tensor_tensor(f[:, s, :], ring[:, POS["rep", t] % 2, :], xs[:, gi % 2, :],
                                        ALU.mult).then_inc(prod_done, 1)

            def low(g, gi, t):
                s = buf(gi, t)
                dve.wait_ge(high_done, tile_n(g, t))
                if t < FULL:
                    nc.vector.tensor_tensor(fl[:, s, :], f[:, s, :], fh[:, s, :], ALU.subtract)\
                      .then_inc(low_dve, 1)
                else:
                    nc.vector.tensor_tensor(fh[96:P, s, :], f[96:P, s, :], fh[96:P, s, :], ALU.subtract)\
                      .then_inc(low_dve, 1)

            def x1_second_half(g):
                dve.wait_ge(acc_done, 2 * g + 2)
                nc.vector.tensor_copy(x1[:, HC:GC], acc[:, 1, :]).then_inc(x1_b, 1)

            def turned_low(g):
                dve.wait_ge(x1t_high, g + 1)
                nc.vector.tensor_tensor(x1tl[:, :, :], ring[:, 0, :].rearrange("p (q h) -> p q h", h=H),
                                        x1th[:, :, :], ALU.subtract).then_inc(x1t_low, 1)

            def g_lows(g, gi, qs):
                for q in qs:
                    dve.wait_ge(g_high, NQ * g + q + 1)
                    nc.vector.tensor_tensor(gl[:, :, g_at(gi, q)], g_psum(q), gh[:, :, g_at(gi, q)],
                                            ALU.subtract).then_inc(g_low, 1)

            def chunk(j, first, last):
                for gi in range(CB):
                    g = CB * j + gi
                    prev = not (first and gi == 0)
                    product(g, gi, 1, first)
                    low(g, gi, 0)
                    if prev:
                        x1_second_half(g - 1)
                    if prev and not (first and gi == 1):
                        g_lows(g - 2, gi - 1, (6, 7))
                    product(g, gi, 2, first)
                    if prev:
                        turned_low(g - 1)
                    low(g, gi, 2)
                    product(g, gi, 3, first)
                    product(g, gi, 4, first)
                    low(g, gi, 4)
                    product(g, gi, 5, first)
                    if prev:
                        g_lows(g - 1, gi, (0, 1))
                    product(g, gi, 6, first)
                    if prev:
                        g_lows(g - 1, gi, (2, 3))
                    low(g, gi, 6)
                    if not (last and gi == CB - 1):
                        product(g + 1, (gi + 1) % CB, 0, False)
                    if prev:
                        g_lows(g - 1, gi, (4, 5))

            dve.wait_ge(consts_in, 48)
            nc.vector.tensor_tensor(f[:, 1, 0:FULL * H], f[:, 1, 0:FULL * H], x1[:, 0:FULL * H], ALU.add)\
              .then_inc(w0_sum, 1)
            dve.wait_ge(w0_high, 2)
            nc.vector.tensor_tensor(w0l[:, 0:FULL, :], f[:, 1, 0:FULL * H].rearrange("p (t h) -> p t h", h=H),
                                    w0h[:, 0:FULL, :], ALU.subtract).then_inc(w0_ready, 1)
            nc.vector.tensor_tensor(x1[:, FULL * H:TILES * H], x1[:, FULL * H:TILES * H], w0l[:, FULL, :],
                                    ALU.subtract).then_inc(w0_sum, 1)
            dve.wait_ge(w0_sum, 2)
            nc.vector.tensor_tensor(w0l[:, FULL, :], x1[:, FULL * H:TILES * H], w0h[:, FULL, :],
                                    ALU.add).then_inc(w0_ready, 1)
            dve.wait_ge(w0_ready, 2)
            dve.wait_ge(sel_ready, 1)
            product(0, 0, 0, True)
            chunk(0, True, False)
            with dve.Fori(1, NCH - 1) as j:
                chunk(j, False, False)
            chunk(NCH - 1, False, True)
            x1_second_half(NG - 1)
            g_lows(NG - 2, CB - 1, (6, 7))
            turned_low(NG - 1)
            g_lows(NG - 1, CB, range(NQ))

        @block.gpsimd
        def _(pool):
            def low(g, gi, t):
                s = buf(gi, t)
                pool.wait_ge(high_done, tile_n(g, t))
                nc.gpsimd.tensor_tensor(fl[:, s, :], f[:, s, :], fh[:, s, :], ALU.subtract)\
                  .then_inc(low_pool, 1)

            def x_split(g, gi):
                pool.wait_ge(x_high, g + 1)
                nc.gpsimd.tensor_tensor(xhl[LO_ROW:P, gi % 2, :], xs[LO_ROW:P, gi % 2, :],
                                        xhl[LO_ROW:P, gi % 2, :], ALU.subtract).then_inc(x_low, 1)

            def xd_split(g):
                pool.wait_ge(xd_high, g + 1)
                nc.gpsimd.tensor_tensor(xdhl[:, :, 1, :], xdr[:, :, :], xdhl[:, :, 0, :], ALU.subtract)\
                  .then_inc(xd_low, 1)

            def w1_piece(p):
                n = min(NW, M - NW * p)
                pool.wait_ge(w1_high, p + 1)
                nc.gpsimd.tensor_tensor(w1l[:, NW * p:NW * p + n, :],
                                        outs[:, :, :].rearrange("p a b -> p (a b)")[:, 0:n * H]
                                        .rearrange("p (n h) -> p n h", h=H),
                                        w1h[:, NW * p:NW * p + n, :], ALU.subtract).then_inc(w1_ready, 1)

            def first_out(c):
                pool.wait_ge(g_high, CB * NQ * (c + 1))
                pool.wait_ge(g_low, CB * NQ * (c + 1))
                pool.wait_ge(w1_ready, PIECES)
                pool.wait_ge(outs_dma, 16 * (c + 1))
                nc.gpsimd.tensor_tensor(outs[:, 0, :], gh[:, M, :], gl[:, M, :], ALU.add)\
                  .then_inc(out1_ready, 1)

            def chunk(j, first, last):
                for gi in range(CB):
                    g = CB * j + gi
                    piece = 3 * gi if first else PIECES
                    low(g, gi, 1)
                    if not (last and gi == CB - 1):
                        pool.wait_ge(low_pool, len(POOL_LO) * g + 1)
                        x_split(g + 1, gi + 1)
                        pool.wait_ge(x_low, g + 2)
                    xd_split(g)
                    if piece < PIECES:
                        w1_piece(piece)
                    low(g, gi, 3)
                    if gi == 1 and not first:
                        first_out(j - 1)
                    if piece + 1 < PIECES:
                        w1_piece(piece + 1)
                    low(g, gi, 5)
                    if piece + 2 < PIECES:
                        w1_piece(piece + 2)

            nc.gpsimd.memset(xbd[:, :, :, :, :].rearrange("p q s b i -> p (q s b i)").bitcast(F32), 0.0)\
              .then_inc(xbd_zero, 1)
            pool.wait_ge(xbd_zero, 1)
            x_split(0, 0)
            chunk(0, True, False)
            with pool.Fori(1, NCH - 1) as j:
                chunk(j, False, False)
            chunk(NCH - 1, False, True)
            first_out(NCH - 1)


def kernel(r_x, L0_rec_W0, L0_rec_W1):
    import concourse.bacc as bacc
    from concourse.bass_utils import run_bass_kernel_spmd

    x = np.asarray(r_x)
    w0 = np.asarray(L0_rec_W0).reshape(M, M, H)
    w1 = np.asarray(L0_rec_W1).reshape(M, H, H)
    xt = x.transpose(1, 0, 2).reshape(M, NG, GC)
    xa = np.ascontiguousarray(xt[np.arange(P) % M].transpose(1, 0, 2))
    xo = np.ones((B * D, MI), x.dtype)
    xo[:, 0:M] = x.transpose(0, 2, 1).reshape(B * D, M)
    xd = np.ascontiguousarray(xo.reshape(NG, NQ, P, MI).transpose(0, 2, 1, 3))
    w0a = np.zeros((P, TILES, H), w0.dtype)
    w0b = np.zeros((P, TILES, H), w0.dtype)
    sel = np.zeros((P, TILES, P), np.float32)
    for t, m, i, j in pair_slots():
        if t < FULL or not LEFT_HI2 <= m < LEFT_LO:
            w0a[m, t] = w0[i, j]
        if i != j or (t == FULL and LEFT_HI2 <= m < LEFT_LO):
            w0b[m, t] = w0[j, i]
        sel[j, t, m] = 1.0
        sel[LO_AT + j, t, m] = 1.0
    arrays = {
        "xa": xa, "xd": xd,
        "w0a": w0a.reshape(P, TILES * H), "w0b": w0b.reshape(P, TILES * H),
        "w1": np.ascontiguousarray(w1.transpose(1, 0, 2)).reshape(P, M * H),
        "sel": sel.reshape(P, TILES * P), "ident": np.eye(P, dtype=np.float32),
    }
    nc = bacc.Bacc("TRN2", target_bir_lowering=False, num_devices=1)
    args = [nc.dram_tensor(f"{n}_dram", a.shape, F32, kind="ExternalInput").ap() for n, a in arrays.items()]
    out = nc.dram_tensor("out_dram", (NCH, P, 2, NB), F32, kind="ExternalOutput").ap()
    build(nc, *args, out)
    r = run_bass_kernel_spmd(nc, [{f"{n}_dram": a for n, a in arrays.items()}], core_ids=[0])
    got = r.results[0]["out_dram"]
    return np.ascontiguousarray(got.transpose(0, 3, 2, 1)).reshape(B, 2 * H)
```

```python
from contextlib import ExitStack

import numpy as np

import concourse.bass as bass
from concourse import mybir

F32 = mybir.dt.float32
F32R = mybir.dt.float32r
ALU = mybir.AluOpType
COPY = mybir.ActivationFunctionType.Copy
SQUARE = mybir.ActivationFunctionType.Square

P = 128
B, M, D = 2048, 39, 16
H = 128
GC = 512
NG = B * D // GC
TILES = 7
FULL = TILES - 1
LEFT = range(18, 30)
LEFT_HI, LEFT_HI2, LEFT_LO = 0, M, 2 * M
NQ = GC // P
BQ = P // D
MI = M + 1
CB = 8
NB = CB * GC // D
NCH = NG // CB
LO_ROW = 64
LO_AT = 2 * M
POOL_LO = (0, 1, 3, 5)
DVE_LO = (2, 4, 6)
NW = 4
PIECES = -(-M // NW)
FILLS = [("rep", t) for t in range(4)] + [("turn", 0)] + [("rep", t) for t in range(4, TILES)]
STEPS = len(FILLS)
POS = {f: k for k, f in enumerate(FILLS)}
RING = 4
AHEAD = 3
G_AT = {4: (0, 1), 5: (2,), 6: (3,)}
XSB = 4
PPG = 2


def pair_slots():
    left = set(LEFT)
    cap = [FULL * len(range(v, P, M)) for v in range(M)]
    own = {(i, i): i for i in range(M) if i not in left}
    for i in range(M):
        for s in range(1, (M + 1) // 2):
            j = (i + s) % M
            own[min(i, j), max(i, j)] = i
    count = [0] * M
    for v in own.values():
        count[v] += 1
    for v in range(M):
        while count[v] < cap[v]:
            back, queue, found = {v: None}, [v], None
            while queue and found is None:
                a = queue.pop(0)
                for u in range(M):
                    if u not in back and own[min(u, a), max(u, a)] == u:
                        back[u] = a
                        queue.append(u)
                        if count[u] > cap[u]:
                            found = u
                            break
            u = found
            while back[u] is not None:
                a = back[u]
                own[min(u, a), max(u, a)] = a
                u = a
            count[found] -= 1
            count[v] += 1
    assert count == cap
    free = {v: [(t, m) for t in range(FULL) for m in range(v, P, M)] for v in range(M)}
    slots = [(*free[v].pop(), v, i + j - v) for (i, j), v in sorted(own.items())]
    for i in LEFT:
        slots += [(FULL, r + i, i, i) for r in (LEFT_HI, LEFT_HI2, LEFT_LO)]
    return slots


def build(nc, xa, xd, w0a, w0b, w1, sel, ident, out):
    with ExitStack() as ctx:
        def sb(name, shape, dt=F32):
            return ctx.enter_context(nc.sbuf_tensor(name, shape, dt))

        def sem(name):
            return ctx.enter_context(nc.semaphore(name))

        w0h = sb("w0h", [P, TILES, H], F32R)
        w0l = sb("w0l", [P, TILES, H], F32R)
        selr = sb("selr", [P, TILES, P], F32R)
        w1h = sb("w1h", [P, M, H], F32R)
        w1l = sb("w1l", [P, M, H], F32R)
        gh = sb("gh", [P, MI, NB], F32R)
        gl = sb("gl", [P, MI, NB], F32R)
        xs = sb("xs", [P, XSB, GC])
        xhl = sb("xhl", [P, 2, GC], F32R)
        f = sb("f", [P, RING, GC])
        fh = sb("fh", [P, RING, GC], F32R)
        fl = sb("fl", [P, RING, GC], F32R)
        x1 = sb("x1", [P, 2, GC])
        x1th = sb("x1th", [P, 2, NQ, H], F32R)
        x1tl = sb("x1tl", [P, 2, NQ, H], F32R)
        xdr = sb("xdr", [P, 2, NQ, MI])
        xdhl = sb("xdhl", [P, 2, NQ, 2, MI], F32R)
        xbd = sb("xbd", [P, 2, NQ, 2, BQ, MI], F32R)
        outs = sb("outs", [P, 2, NB])
        idn = sb("idn", [P, P])
        ring = ctx.enter_context(nc.psum_tensor("ring", [P, RING, GC], F32))
        acc = ctx.enter_context(nc.psum_tensor("acc", [P, 2, GC], F32))
        pg = ctx.enter_context(nc.psum_tensor("pg", [P, 2, GC], F32))
        f_flat = f[:, :, :].rearrange("p s c -> p (s c)")
        x1_flat = x1[:, :, :].rearrange("p s c -> p (s c)")
        sel_raw = f_flat[:, 0:TILES * P]
        w0a_raw = f_flat[:, 2 * GC:2 * GC + TILES * H]
        w0b_raw = x1_flat[:, 0:TILES * H]

        consts_in = sem("consts_in")
        ident_in = sem("ident_in")
        sel_ready = sem("sel_ready")
        w0_sum = sem("w0_sum")
        w0_high = sem("w0_high")
        w0_ready = sem("w0_ready")
        xbd_zero = sem("xbd_zero")
        w1_in = sem("w1_in")
        w1_high = sem("w1_high")
        w1_ready = sem("w1_ready")
        xs_in = [sem(f"xs_in{n}") for n in range(XSB)]
        x_high = sem("x_high")
        x_low = sem("x_low")
        xd_in = [sem("xd_in0"), sem("xd_in1")]
        xd_high = sem("xd_high")
        xd_low = sem("xd_low")
        xbd_in = [sem("xbd_in0"), sem("xbd_in1")]
        rep_done = sem("rep_done")
        prod_done = sem("prod_done")
        high_done = sem("high_done")
        low_dve = sem("low_dve")
        low_pool = sem("low_pool")
        main_done = sem("main_done")
        x1_ready = sem("x1_ready")
        turned = sem("turned")
        x1t_high = sem("x1t_high")
        x1t_low = sem("x1t_low")
        g_done = sem("g_done")
        g_high = sem("g_high")
        g_low = sem("g_low")
        fin_done = sem("fin_done")
        out1_ready = sem("out1_ready")
        out2_ready = sem("out2_ready")
        outs_dma = sem("outs_dma")

        def tile_n(g, t):
            return TILES * g + t + 1

        def full_n(g, t):
            return FULL * g + t + 1

        def nth(j, gi, bufs):
            return CB // bufs * j + gi // bufs + 1

        def wait_used(eng, g, t):
            if t < FULL:
                eng.wait_ge(prod_done, full_n(g, t))
            else:
                eng.wait_ge(high_done, tile_n(g, t))

        def wait_low(eng, g, t):
            if t in POOL_LO:
                eng.wait_ge(low_pool, len(POOL_LO) * g + POOL_LO.index(t) + 1)
            else:
                eng.wait_ge(low_dve, len(DVE_LO) * g + DVE_LO.index(t) + 1)

        def buf(gi, t):
            return (TILES * gi + t) % RING

        def before(gi, t, back):
            n = t - back
            return (0, n) if n >= 0 else (-1, n + TILES)

        def g_at(gi, q):
            b0 = ((gi - 1) % CB) * (NB // CB) + q * BQ
            return slice(b0, b0 + BQ)

        def g_psum(q):
            return pg[:, q % 2, 0:BQ * MI].rearrange("p (b i) -> p i b", b=BQ)

        block = ctx.enter_context(nc.Block())

        @block.sync
        def _(sp):
            def load_x(j, gi):
                sp.dma_start(xs[:, gi % XSB, :], xa[CB * j + gi]).then_inc(xs_in[gi % XSB], 16)

            def load_xd(j, gi):
                sp.dma_start(xdr[:, gi % 2, :, :], xd[CB * j + gi]).then_inc(xd_in[gi % 2], 16)

            def w1_load(p):
                n = min(NW, M - NW * p)
                if p:
                    sp.wait_ge(w1_ready, p)
                sp.dma_start(outs[:, :, :].rearrange("p a b -> p (a b)")[:, 0:n * H],
                             w1[:, NW * p * H:(NW * p + n) * H])\
                  .then_inc(w1_in if p < PIECES - 1 else outs_dma, 16)

            def blocks(g, gi, first):
                sp.wait_ge(xd_low, g + 1)
                if first:
                    sp.wait_ge(xbd_zero, 1)
                else:
                    sp.wait_ge(turned, g)
                s = gi % 2
                for b in range(BQ):
                    rows = slice(D * b, D * b + D)
                    sp.dma_start(xbd[rows, s, :, :, b, :].rearrange("p q s i -> p (q s) i").bitcast(F32),
                                 xdhl[rows, s, :, :, :].rearrange("p q s i -> p (q s) i").bitcast(F32))\
                      .then_inc(xbd_in[s], 16)

            def send(c):
                sp.wait_ge(out1_ready, c + 1)
                sp.wait_ge(out2_ready, c + 1)
                sp.dma_start(out[c], outs[:, :, :]).then_inc(outs_dma, 16)

            def chunk(j, first, last):
                for gi in range(CB):
                    g = CB * j + gi
                    if not (last and gi + XSB - 1 >= CB):
                        if not (first and gi == 0):
                            sp.wait_ge(prod_done, FULL * g)
                            sp.wait_ge(x_low, g)
                        load_x(j, gi + XSB - 1)
                    blocks(g, gi, first and gi < 2)
                    if not (last and gi + 2 >= CB):
                        load_xd(j, gi + 2)
                    if gi == 2 and not first:
                        send(j - 1)
                    if first:
                        for p in range(PPG * gi + 1, min(PPG * (gi + 1) + 1, PIECES)):
                            w1_load(p)

            load_x(0, 0)
            sp.dma_start(sel_raw, sel).then_inc(consts_in, 16)
            sp.dma_start(w0a_raw, w0a).then_inc(consts_in, 16)
            sp.dma_start(w0b_raw, w0b).then_inc(consts_in, 16)
            load_xd(0, 0)
            load_xd(0, 1)
            sp.dma_start(idn[:, :], ident).then_inc(ident_in, 16)
            load_x(0, 1)
            load_x(0, 2)
            w1_load(0)
            chunk(0, True, False)
            with sp.Fori(1, NCH - 1) as j:
                chunk(j, False, False)
            chunk(NCH - 1, False, True)
            send(NCH - 1)
            sp.wait_ge(outs_dma, 16 * (NCH + 1))

        @block.tensor
        def _(pe):
            def fill_rep(g, gi, t, slot):
                if t == 0:
                    pe.wait_ge(x_high, g + 1)
                    pe.wait_ge(x_low, g + 1)
                nc.tensor.matmul(ring[:, slot, :], selr[:, t, :], xhl[:, gi % 2, :],
                                 start=True, stop=True).then_inc(rep_done, 1)

            def fill_turn(g, gi, slot):
                pe.wait_ge(x1_ready, g + 1)
                for q in range(NQ):
                    last = nc.tensor.transpose(ring[:, slot, q * H:(q + 1) * H],
                                               x1[:, gi % 2, q * P:(q + 1) * P], idn[:, :])
                last.then_inc(turned, 1)

            def fill(g, gi, k, first):
                kind, t = FILLS[k]
                if first and gi == 0 and kind == "turn":
                    return
                if k >= RING:
                    wait_used(pe, g, FILLS[k - RING][1])
                elif FILLS[k + STEPS - RING][0] == "rep":
                    if not (first and gi == 0):
                        wait_used(pe, g - 1, FILLS[k + STEPS - RING][1])
                elif first and gi == 1:
                    wait_used(pe, 0, FILLS[k][1])
                elif not (first and gi == 0):
                    pe.wait_ge(x1t_low, g - 1)
                if kind == "rep":
                    fill_rep(g, gi, t, k % RING)
                else:
                    fill_turn(g - 1, gi - 1, k % RING)

            def main(g, gi, t, fresh):
                if t == 0 and not fresh:
                    pe.wait_ge(x1_ready, g - 1)
                pe.wait_ge(high_done, tile_n(g, t))
                wait_low(pe, g, t)
                s, o = buf(gi, t), acc[:, gi % 2, :]
                if t < FULL:
                    nc.tensor.matmul(o, w0h[:, t, :], fh[:, s, :], start=t == 0, stop=False)
                    nc.tensor.matmul(o, w0l[:, t, :], fh[:, s, :], start=False, stop=False)
                    nc.tensor.matmul(o, w0h[:, t, :], fl[:, s, :], start=False, stop=False)\
                      .then_inc(main_done, 1)
                else:
                    nc.tensor.matmul(o, w0l[:, t, :], fh[:, s, :], start=False, stop=True)\
                      .then_inc(main_done, 1)

            def g_tile(j, g, gi, q, fresh, after_final):
                s = gi % 2
                if q == 0:
                    pe.wait_ge(x1t_low, g + 1)
                    pe.wait_ge(xbd_in[s], 16 * BQ * nth(j, gi, 2))
                    if after_final is not None:
                        pe.wait_ge(out2_ready, after_final)
                if not (fresh and q < 2):
                    pe.wait_ge(g_low, NQ * g + q - 1)
                o = pg[:, q % 2, 0:BQ * MI]
                xh = xbd[:, s, q, 0, :, :].rearrange("p b i -> p (b i)")
                xl = xbd[:, s, q, 1, :, :].rearrange("p b i -> p (b i)")
                nc.tensor.matmul(o, x1th[:, s, q, :], xh, start=True, stop=False)
                nc.tensor.matmul(o, x1th[:, s, q, :], xl, start=False, stop=False)
                nc.tensor.matmul(o, x1tl[:, s, q, :], xh, start=False, stop=True).then_inc(g_done, 1)

            def final(c):
                pe.wait_ge(g_low, CB * NQ * (c + 1))
                pe.wait_ge(w1_ready, PIECES)
                o = pg[:, 0, 0:NB]
                for i in range(M):
                    nc.tensor.matmul(o, w1h[:, i, :], gh[:, i, :], start=i == 0, stop=False)
                    nc.tensor.matmul(o, w1l[:, i, :], gh[:, i, :], start=False, stop=False)
                    last = nc.tensor.matmul(o, w1h[:, i, :], gl[:, i, :], start=False, stop=i == M - 1)
                last.then_inc(fin_done, 1)

            def chunk(j, first, last):
                for gi in range(CB):
                    g = CB * j + gi
                    for k in range(STEPS):
                        if k + AHEAD < STEPS:
                            fill(g, gi, k + AHEAD, first)
                        elif not (last and gi == CB - 1):
                            fill(g + 1, gi + 1, k + AHEAD - STEPS, first)
                        kind, t = FILLS[k]
                        if kind == "rep":
                            main(g, gi, t, first and gi < 2)
                        if not (first and gi == 0):
                            for q in G_AT.get(k, ()):
                                g_tile(j, g - 1, gi - 1, q, first and gi == 1,
                                       j if gi == 1 and not first else None)
                        if k == 0 and gi == 1 and not first:
                            final(j - 1)

            pe.wait_ge(sel_ready, 1)
            for k in range(AHEAD):
                fill(0, 0, k, True)
            pe.wait_ge(w0_ready, 2)
            pe.wait_ge(ident_in, 16)
            chunk(0, True, False)
            with pe.Fori(1, NCH - 1) as j:
                chunk(j, False, False)
            chunk(NCH - 1, False, True)
            fill_turn(NG - 1, CB - 1, POS["turn", 0] % RING)
            for q in range(NQ):
                g_tile(NCH - 1, NG - 1, CB - 1, q, False, None)
            final(NCH - 1)

        @block.scalar
        def _(act):
            def high(g, gi, t, first):
                s = buf(gi, t)
                if not (first and gi == 0 and t < RING):
                    dg, dt = before(gi, t, RING)
                    act.wait_ge(main_done, tile_n(g + dg, dt))
                if t < FULL:
                    act.wait_ge(prod_done, full_n(g, t))
                    nc.scalar.activation(fh[:, s, :], f[:, s, :], COPY).then_inc(high_done, 1)
                else:
                    r = ring[:, POS["rep", t] % RING, :]
                    act.wait_ge(rep_done, tile_n(g, t))
                    nc.scalar.activation(f[96:P, s, :], r[96:P, :], SQUARE)
                    nc.scalar.activation(fh[:, s, :], r, SQUARE).then_inc(high_done, 1)

            def x1_out(g, gi):
                act.wait_ge(main_done, tile_n(g, FULL))
                nc.scalar.activation(x1[:, gi % 2, :], acc[:, gi % 2, :], COPY).then_inc(x1_ready, 1)

            def x_split(j, gi, first):
                g = CB * j + gi
                act.wait_ge(xs_in[gi % XSB], 16 * nth(j, gi, XSB))
                if not first:
                    act.wait_ge(rep_done, TILES * (g - 1))
                nc.scalar.activation(xhl[:, gi % 2, :], xs[:, gi % XSB, :], COPY).then_inc(x_high, 1)

            def xd_split(j, gi, first):
                g = CB * j + gi
                act.wait_ge(xd_in[gi % 2], 16 * nth(j, gi, 2))
                if not first:
                    act.wait_ge(xbd_in[gi % 2], 16 * BQ * (nth(j, gi, 2) - 1))
                nc.scalar.activation(xdhl[:, gi % 2, :, 0, :], xdr[:, gi % 2, :, :], COPY).then_inc(xd_high, 1)

            def turned_high(g, gi):
                act.wait_ge(turned, g + 1)
                nc.scalar.activation(x1th[:, gi % 2, :, :],
                                     ring[:, POS["turn", 0] % RING, :].rearrange("p (q h) -> p q h", h=H), COPY)\
                  .then_inc(x1t_high, 1)

            def g_high_part(g, gi, q, freed):
                act.wait_ge(g_done, NQ * g + q + 1)
                if q == 0 and freed is not None:
                    act.wait_ge(fin_done, freed)
                    act.wait_ge(out1_ready, freed)
                nc.scalar.activation(gh[:, :, g_at(gi + 1, q)], g_psum(q), COPY).then_inc(g_high, 1)

            def final_out(c):
                act.wait_ge(fin_done, c + 1)
                act.wait_ge(outs_dma, 16 * (c + 1))
                nc.scalar.activation(outs[:, 1, :], pg[:, 0, 0:NB], COPY).then_inc(out2_ready, 1)

            def w1_piece(p):
                n = min(NW, M - NW * p)
                if p < PIECES - 1:
                    act.wait_ge(w1_in, 16 * (p + 1))
                else:
                    act.wait_ge(outs_dma, 16)
                nc.scalar.activation(w1h[:, NW * p:NW * p + n, :],
                                     outs[:, :, :].rearrange("p a b -> p (a b)")[:, 0:n * H], COPY)\
                  .then_inc(w1_high, 1)

            def chunk(j, first, last):
                for gi in range(CB):
                    g = CB * j + gi
                    prev = not (first and gi == 0)
                    more = not (last and gi == CB - 1)
                    piece = PPG * gi if first else PIECES
                    high(g, gi, 0, first)
                    if prev and not (first and gi == 1):
                        g_high_part(g - 2, gi - 2, 3, None)
                    high(g, gi, 1, first)
                    if prev:
                        x1_out(g - 1, gi - 1)
                    if more:
                        x_split(j, gi + 1, first and gi == 0)
                    high(g, gi, 2, first)
                    if gi == 1 and not first:
                        final_out(j - 1)
                    if more:
                        xd_split(j, gi + 1, first and gi == 0)
                    high(g, gi, 3, first)
                    if prev:
                        turned_high(g - 1, gi - 1)
                    if piece < PIECES:
                        w1_piece(piece)
                    high(g, gi, 4, first)
                    high(g, gi, 5, first)
                    if prev:
                        g_high_part(g - 1, gi - 1, 0, j if gi == 1 and not first else None)
                        g_high_part(g - 1, gi - 1, 1, None)
                    if piece + 1 < PIECES:
                        w1_piece(piece + 1)
                    high(g, gi, 6, first)
                    if prev:
                        g_high_part(g - 1, gi - 1, 2, None)

            x_split(0, 0, True)
            xd_split(0, 0, True)
            act.wait_ge(consts_in, 48)
            nc.scalar.activation(selr[:, :, :], sel_raw.rearrange("p (t m) -> p t m", m=P), COPY)\
              .then_inc(sel_ready, 1)
            act.wait_ge(w0_sum, 1)
            nc.scalar.activation(w0h[:, :, :], w0a_raw.rearrange("p (t h) -> p t h", h=H), COPY)\
              .then_inc(w0_high, 1)
            nc.scalar.activation(w0l[:, FULL, :], w0b_raw[:, FULL * H:TILES * H], COPY).then_inc(w0_high, 1)
            chunk(0, True, False)
            with act.Fori(1, NCH - 1) as j:
                chunk(j, False, False)
            chunk(NCH - 1, False, True)
            g_high_part(NG - 2, CB - 2, 3, None)
            x1_out(NG - 1, CB - 1)
            turned_high(NG - 1, CB - 1)
            for q in range(NQ):
                g_high_part(NG - 1, CB - 1, q, None)
            final_out(NCH - 1)

        @block.vector
        def _(dve):
            def product(g, gi, t, first):
                s = buf(gi, t)
                dve.wait_ge(rep_done, tile_n(g, t))
                if not (first and gi == 0 and t < RING):
                    dg, dt = before(gi, t, RING)
                    dve.wait_ge(high_done, tile_n(g + dg, dt))
                    wait_low(dve, g + dg, dt)
                nc.vector.tensor_tensor(f[:, s, :], ring[:, POS["rep", t] % RING, :], xs[:, gi % XSB, :],
                                        ALU.mult).then_inc(prod_done, 1)

            def low(g, gi, t):
                s = buf(gi, t)
                dve.wait_ge(high_done, tile_n(g, t))
                if t < FULL:
                    nc.vector.tensor_tensor(fl[:, s, :], f[:, s, :], fh[:, s, :], ALU.subtract)\
                      .then_inc(low_dve, 1)
                else:
                    nc.vector.tensor_tensor(fh[96:P, s, :], f[96:P, s, :], fh[96:P, s, :], ALU.subtract)\
                      .then_inc(low_dve, 1)

            def turned_low(g, gi):
                dve.wait_ge(x1t_high, g + 1)
                nc.vector.tensor_tensor(x1tl[:, gi % 2, :, :],
                                        ring[:, POS["turn", 0] % RING, :].rearrange("p (q h) -> p q h", h=H),
                                        x1th[:, gi % 2, :, :], ALU.subtract).then_inc(x1t_low, 1)

            def g_low_part(g, gi, q):
                dve.wait_ge(g_high, NQ * g + q + 1)
                nc.vector.tensor_tensor(gl[:, :, g_at(gi + 1, q)], g_psum(q), gh[:, :, g_at(gi + 1, q)],
                                        ALU.subtract).then_inc(g_low, 1)

            def chunk(j, first, last):
                for gi in range(CB):
                    g = CB * j + gi
                    prev = not (first and gi == 0)
                    product(g, gi, 1, first)
                    if prev and not (first and gi == 1):
                        g_low_part(g - 2, gi - 2, 3)
                    product(g, gi, 2, first)
                    product(g, gi, 3, first)
                    low(g, gi, 2)
                    product(g, gi, 4, first)
                    if prev:
                        turned_low(g - 1, gi - 1)
                    low(g, gi, 4)
                    product(g, gi, 5, first)
                    if prev:
                        g_low_part(g - 1, gi - 1, 0)
                        g_low_part(g - 1, gi - 1, 1)
                    if not (last and gi == CB - 1):
                        product(g + 1, gi + 1, 0, first)
                    low(g, gi, 6)
                    if prev:
                        g_low_part(g - 1, gi - 1, 2)

            dve.wait_ge(consts_in, 48)
            nc.vector.tensor_tensor(w0a_raw[:, 0:FULL * H], w0a_raw[:, 0:FULL * H], w0b_raw[:, 0:FULL * H],
                                    ALU.add).then_inc(w0_sum, 1)
            dve.wait_ge(w0_high, 2)
            nc.vector.tensor_tensor(w0l[:, 0:FULL, :], w0a_raw[:, 0:FULL * H].rearrange("p (t h) -> p t h", h=H),
                                    w0h[:, 0:FULL, :], ALU.subtract).then_inc(w0_ready, 1)
            nc.vector.tensor_tensor(w0b_raw[:, FULL * H:TILES * H], w0b_raw[:, FULL * H:TILES * H],
                                    w0l[:, FULL, :], ALU.subtract).then_inc(w0_sum, 1)
            dve.wait_ge(w0_sum, 2)
            nc.vector.tensor_tensor(w0l[:, FULL, :], w0b_raw[:, FULL * H:TILES * H], w0h[:, FULL, :],
                                    ALU.add).then_inc(w0_ready, 1)
            dve.wait_ge(w0_ready, 2)
            dve.wait_ge(sel_ready, 1)
            product(0, 0, 0, True)
            chunk(0, True, False)
            with dve.Fori(1, NCH - 1) as j:
                chunk(j, False, False)
            chunk(NCH - 1, False, True)
            g_low_part(NG - 2, CB - 2, 3)
            turned_low(NG - 1, CB - 1)
            for q in range(NQ):
                g_low_part(NG - 1, CB - 1, q)

        @block.gpsimd
        def _(pool):
            def low(g, gi, t):
                s = buf(gi, t)
                pool.wait_ge(high_done, tile_n(g, t))
                nc.gpsimd.tensor_tensor(fl[:, s, :], f[:, s, :], fh[:, s, :], ALU.subtract)\
                  .then_inc(low_pool, 1)

            def x_split(g, gi):
                pool.wait_ge(x_high, g + 1)
                nc.gpsimd.tensor_tensor(xhl[LO_ROW:P, gi % 2, :], xs[LO_ROW:P, gi % XSB, :],
                                        xhl[LO_ROW:P, gi % 2, :], ALU.subtract).then_inc(x_low, 1)

            def xd_split(g, gi):
                pool.wait_ge(xd_high, g + 1)
                nc.gpsimd.tensor_tensor(xdhl[:, gi % 2, :, 1, :], xdr[:, gi % 2, :, :], xdhl[:, gi % 2, :, 0, :],
                                        ALU.subtract).then_inc(xd_low, 1)

            def w1_piece(p):
                n = min(NW, M - NW * p)
                pool.wait_ge(w1_high, p + 1)
                nc.gpsimd.tensor_tensor(w1l[:, NW * p:NW * p + n, :],
                                        outs[:, :, :].rearrange("p a b -> p (a b)")[:, 0:n * H]
                                        .rearrange("p (n h) -> p n h", h=H),
                                        w1h[:, NW * p:NW * p + n, :], ALU.subtract).then_inc(w1_ready, 1)

            def first_out(c):
                pool.wait_ge(g_low, CB * NQ * (c + 1))
                pool.wait_ge(outs_dma, 16 * (c + 1))
                nc.gpsimd.tensor_tensor(outs[:, 0, :], gh[:, M, :], gl[:, M, :], ALU.add)\
                  .then_inc(out1_ready, 1)

            def chunk(j, first, last):
                for gi in range(CB):
                    g = CB * j + gi
                    more = not (last and gi == CB - 1)
                    piece = PPG * gi if first else PIECES
                    low(g, gi, 0)
                    low(g, gi, 1)
                    if more:
                        pool.wait_ge(low_pool, len(POOL_LO) * g + 2)
                        x_split(g + 1, gi + 1)
                        pool.wait_ge(x_low, g + 2)
                        xd_split(g + 1, gi + 1)
                    low(g, gi, 3)
                    if piece < PIECES:
                        w1_piece(piece)
                    if gi == 1 and not first:
                        first_out(j - 1)
                    low(g, gi, 5)
                    if piece + 1 < PIECES:
                        w1_piece(piece + 1)

            nc.gpsimd.memset(xbd[:, :, :, :, :, :].rearrange("p u q s b i -> p (u q s b i)").bitcast(F32), 0.0)\
              .then_inc(xbd_zero, 1)
            pool.wait_ge(xbd_zero, 1)
            x_split(0, 0)
            pool.wait_ge(x_low, 1)
            xd_split(0, 0)
            chunk(0, True, False)
            with pool.Fori(1, NCH - 1) as j:
                chunk(j, False, False)
            chunk(NCH - 1, False, True)
            first_out(NCH - 1)


def kernel(r_x, L0_rec_W0, L0_rec_W1):
    import concourse.bacc as bacc
    from concourse.bass_utils import run_bass_kernel_spmd

    x = np.asarray(r_x)
    w0 = np.asarray(L0_rec_W0).reshape(M, M, H)
    w1 = np.asarray(L0_rec_W1).reshape(M, H, H)
    xt = x.transpose(1, 0, 2).reshape(M, NG, GC)
    xa = np.ascontiguousarray(xt[np.arange(P) % M].transpose(1, 0, 2))
    xo = np.ones((B * D, MI), x.dtype)
    xo[:, 0:M] = x.transpose(0, 2, 1).reshape(B * D, M)
    xd = np.ascontiguousarray(xo.reshape(NG, NQ, P, MI).transpose(0, 2, 1, 3))
    w0a = np.zeros((P, TILES, H), w0.dtype)
    w0b = np.zeros((P, TILES, H), w0.dtype)
    sel = np.zeros((P, TILES, P), np.float32)
    for t, m, i, j in pair_slots():
        if t < FULL or not LEFT_HI2 <= m < LEFT_LO:
            w0a[m, t] = w0[i, j]
        if i != j or (t == FULL and LEFT_HI2 <= m < LEFT_LO):
            w0b[m, t] = w0[j, i]
        sel[j, t, m] = 1.0
        sel[LO_AT + j, t, m] = 1.0
    arrays = {
        "xa": xa, "xd": xd,
        "w0a": w0a.reshape(P, TILES * H), "w0b": w0b.reshape(P, TILES * H),
        "w1": np.ascontiguousarray(w1.transpose(1, 0, 2)).reshape(P, M * H),
        "sel": sel.reshape(P, TILES * P), "ident": np.eye(P, dtype=np.float32),
    }
    nc = bacc.Bacc("TRN2", target_bir_lowering=False, num_devices=1)
    args = [nc.dram_tensor(f"{n}_dram", a.shape, F32, kind="ExternalInput").ap() for n, a in arrays.items()]
    out = nc.dram_tensor("out_dram", (NCH, P, 2, NB), F32, kind="ExternalOutput").ap()
    build(nc, *args, out)
    r = run_bass_kernel_spmd(nc, [{f"{n}_dram": a for n, a in arrays.items()}], core_ids=[0])
    got = r.results[0]["out_dram"]
    return np.ascontiguousarray(got.transpose(0, 3, 2, 1)).reshape(B, 2 * H)
```

```python
from contextlib import ExitStack

import numpy as np

import concourse.bass as bass
from concourse import mybir

F32 = mybir.dt.float32
F32R = mybir.dt.float32r
ALU = mybir.AluOpType
COPY = mybir.ActivationFunctionType.Copy
SQUARE = mybir.ActivationFunctionType.Square

P = 128
B, M, D = 2048, 39, 16
H = 128
GC = 512
NG = B * D // GC
TILES = 7
FULL = TILES - 1
LEFT = range(18, 30)
PICKED = range(14, 34)
SUB = 32
LO_ROW = 2 * SUB
NQ = GC // P
BQ = P // D
MI = M + 1
CB = 8
NB = CB * GC // D
NCH = NG // CB
REP = (0, 2, 4)
LOADED = (1, 3, 5)
WHOLE = (1, 3)
SPLIT = (0, 2, 4, 5)
POOL_PROD = (1, 3)
DVE_PROD = (0, 2, 4, 5)
POOL_LOW = (5,)
DVE_LOW = (0, 2, 4)
BUF = (0, 1, 0, 2)
SHARES = {0: (-1, 4), 4: (0, 0)}
ORDER = (*SPLIT, FULL, FULL, *WHOLE)
MAINS = [0, 1, 2, 3, None, 4, 5, FULL]
NW = 4
PIECES = -(-M // NW)
STEPS = len(MAINS)
SLOT = {0: 0, 2: 1, "turn": 2, 4: 3}
FILL_AT = {2: ("turn", 0, 2), 4: (4,)}
RING = 4
G_AT = {4: (0, 1), 6: (2,), 7: (3,)}
XSB = 2
CP = CB // 2
FINAL_AT = 2
EARLY = 2


def pieces_of(gi):
    extra = PIECES - CB
    return range(gi + min(gi, extra), gi + 1 + min(gi + 1, extra))


def pair_slots():
    pairs = [(i, j) for i in range(M) for j in range(i, M) if i != j or i not in LEFT]
    cap = {(v, r): len(range(v, P, M)) * (len(REP) if r else len(LOADED)) for v in range(M) for r in (0, 1)}
    held = {place: [] for place in cap}

    def options(pair):
        for v, w in {pair, pair[::-1]}:
            yield v, 0
            if w in PICKED:
                yield v, 1

    def settle(pair, tried):
        for place in options(pair):
            if place in tried:
                continue
            tried.add(place)
            if len(held[place]) < cap[place]:
                held[place].append(pair)
                return True
            for other in held[place]:
                if settle(other, tried):
                    held[place].remove(other)
                    held[place].append(pair)
                    return True
        return False

    for pair in pairs:
        assert settle(pair, set())
    free = {(v, r): [(t, m) for t in (REP if r else LOADED) for m in range(v, P, M)] for v, r in cap}
    return [(*free[v, r].pop(), v, i + j - v) for (v, r), got in held.items() for i, j in sorted(got)]


def left_rows(u):
    n = len(PICKED)
    for k, i in enumerate(LEFT):
        yield SUB * u + PICKED.index(i), i, "high"
        yield SUB * u + n + k, i, "weight's low"
        yield LO_ROW + SUB * u + PICKED.index(i), i, "low"


def build(nc, xa, xb, xd, xpairs, w0a, w0b, w1, sel, ident, out):
    with ExitStack() as ctx:
        def sb(name, shape, dt=F32):
            return ctx.enter_context(nc.sbuf_tensor(name, shape, dt))

        def sem(name):
            return ctx.enter_context(nc.semaphore(name))

        w0h = sb("w0h", [P, len(SPLIT), H], F32R)
        w0l = sb("w0l", [P, len(SPLIT), H], F32R)
        w0q = sb("w0q", [P, 2, H], F32R)
        w0w = sb("w0w", [P, len(WHOLE), H])
        selr = sb("selr", [P, 2, len(REP), P], F32R)
        w1h = sb("w1h", [P, M, H], F32R)
        w1l = sb("w1l", [P, M, H], F32R)
        gh = sb("gh", [P, MI, NB], F32R)
        gl = sb("gl", [P, MI, NB], F32R)
        xs = sb("xs", [P, XSB, GC])
        xp = sb("xp", [P, 2, GC])
        xhl = sb("xhl", [P, GC], F32R)
        sq = sb("sq", [P, GC], F32R)
        xr = sb("xr", [P, 2, len(LOADED), GC])
        f = sb("f", [P, max(BUF) + 1, GC])
        fh = sb("fh", [P, len(SPLIT), GC], F32R)
        fl = sb("fl", [P, max(BUF) + 1, GC], F32R)
        fw = sb("fw", [P, len(WHOLE), GC])
        x1 = sb("x1", [P, GC])
        x1th = sb("x1th", [P, NQ, H], F32R)
        x1tl = sb("x1tl", [P, NQ, H], F32R)
        xdr = sb("xdr", [P, NQ, MI])
        xdhl = sb("xdhl", [P, 2, NQ, 2, MI], F32R)
        xbd = sb("xbd", [P, 2, NQ, 2, BQ, MI], F32R)
        outs = sb("outs", [P, 2, NB])
        idn = sb("idn", [P, P])
        ring = ctx.enter_context(nc.psum_tensor("ring", [P, RING, GC], F32))
        acc = ctx.enter_context(nc.psum_tensor("acc", [P, 2, GC], F32))
        pg = ctx.enter_context(nc.psum_tensor("pg", [P, 2, GC], F32))
        f_flat = f[:, :, :].rearrange("p s c -> p (s c)")
        xr_flat = xr[:, 1, :, :].rearrange("p s c -> p (s c)")
        sel_raw = f_flat[:, 0:2 * len(REP) * P]
        w0a_raw = xr_flat[:, 0:len(ORDER) * H]
        w0b_raw = fw[:, :, :].rearrange("p s c -> p (s c)")[:, 0:len(ORDER) * H]

        consts_in = sem("consts_in")
        ident_in = sem("ident_in")
        sel_ready = sem("sel_ready")
        w0_sum = sem("w0_sum")
        w0_high = sem("w0_high")
        w0_ready = sem("w0_ready")
        xbd_zero = sem("xbd_zero")
        w1_in = sem("w1_in")
        w1_high = sem("w1_high")
        w1_ready = sem("w1_ready")
        xs_in = [sem(f"xs_in{n}") for n in range(XSB)]
        xp_in = [sem("xp_in0"), sem("xp_in1")]
        x_high = sem("x_high")
        x_low = sem("x_low")
        xr_in = [sem("xr_in0"), sem("xr_in1")]
        sq_high = sem("sq_high")
        sq_ready = sem("sq_ready")
        xd_in = sem("xd_in")
        xd_high = sem("xd_high")
        xd_low = sem("xd_low")
        xbd_in = [sem("xbd_in0"), sem("xbd_in1")]
        rep_done = sem("rep_done")
        prod_dve = sem("prod_dve")
        prod_pool = sem("prod_pool")
        high_done = sem("high_done")
        low_dve = sem("low_dve")
        low_pool = sem("low_pool")
        main_done = sem("main_done")
        x1_ready = sem("x1_ready")
        turned = sem("turned")
        x1t_high = sem("x1t_high")
        x1t_low = sem("x1t_low")
        g_done = sem("g_done")
        g_high = sem("g_high")
        g_low = sem("g_low")
        fin_done = sem("fin_done")
        out1_ready = sem("out1_ready")
        out2_ready = sem("out2_ready")
        outs_dma = sem("outs_dma")

        def tile_n(g, t):
            return TILES * g + t + 1

        def nth_of(tiles, g, t):
            return len(tiles) * g + tiles.index(t) + 1

        def nth(j, gi, bufs):
            return CB // bufs * j + gi // bufs + 1

        def wait_product(eng, g, t):
            if t in POOL_PROD:
                eng.wait_ge(prod_pool, nth_of(POOL_PROD, g, t))
            else:
                eng.wait_ge(prod_dve, nth_of(DVE_PROD, g, t))

        def wait_high(eng, g, t):
            eng.wait_ge(high_done, nth_of(SPLIT, g, t))

        def wait_low(eng, g, t):
            if t in POOL_LOW:
                eng.wait_ge(low_pool, nth_of(POOL_LOW, g, t))
            else:
                eng.wait_ge(low_dve, nth_of(DVE_LOW, g, t))

        def wait_f_free(eng, g, gi, t, first):
            if t in WHOLE:
                if not (first and gi == 0):
                    eng.wait_ge(main_done, tile_n(g - 1, t))
                return
            dg, dt = SHARES.get(t, (-1, t))
            if not (first and gi == 0 and dg < 0):
                wait_high(eng, g + dg, dt)
                wait_low(eng, g + dg, dt)

        def wait_fl_free(eng, g, gi, t, first):
            dg, dt = SHARES.get(t, (-1, t))
            if not (first and gi == 0 and dg < 0):
                eng.wait_ge(main_done, tile_n(g + dg, dt))

        def g_at(gi, q):
            b0 = (gi % CB) * (NB // CB) + q * BQ
            return slice(b0, b0 + BQ)

        def g_psum(q):
            return pg[:, q % 2, 0:BQ * MI].rearrange("p (b i) -> p i b", b=BQ)

        block = ctx.enter_context(nc.Block())

        @block.sync
        def _(sp):
            def load_x(j, gi):
                sp.dma_start(xs[:, gi % XSB, :], xa[CB * j + gi]).then_inc(xs_in[gi % XSB], 16)

            def load_right(j, gi):
                sp.dma_start(xr[:, gi % 2, :, :], xb[CB * j + gi]).then_inc(xr_in[gi % 2], 16)

            def load_pair(j, pi):
                sp.dma_start(xp[:, pi % 2, :], xpairs[CP * j + pi]).then_inc(xp_in[pi % 2], 16)

            def load_xd(g):
                sp.dma_start(xdr[:, :, :], xd[g]).then_inc(xd_in, 16)

            def w1_load(p):
                n = min(NW, M - NW * p)
                if p:
                    sp.wait_ge(w1_ready, p)
                sp.dma_start(outs[:, :, :].rearrange("p a b -> p (a b)")[:, 0:n * H],
                             w1[:, NW * p * H:(NW * p + n) * H])\
                  .then_inc(w1_in if p < PIECES - 1 else outs_dma, 16)

            def blocks(gi, first, some):
                if first:
                    sp.wait_ge(xbd_zero, 1)
                s = gi % 2
                for b in some:
                    rows = slice(D * b, D * b + D)
                    sp.dma_start(xbd[rows, s, :, :, b, :].rearrange("p q s i -> p (q s) i").bitcast(F32),
                                 xdhl[rows, s, :, :, :].rearrange("p q s i -> p (q s) i").bitcast(F32))\
                      .then_inc(xbd_in[s], 16)

            def send(c):
                sp.wait_ge(out1_ready, c + 1)
                sp.wait_ge(out2_ready, c + 1)
                sp.dma_start(out[c], outs[:, :, :]).then_inc(outs_dma, 16)

            def chunk(j, first, last):
                for gi in range(CB):
                    g = CB * j + gi
                    sp.wait_ge(xd_low, g + 1)
                    if not (last and gi + 1 >= CB):
                        load_xd(g + 1)
                    if not (first and gi == 0):
                        sp.wait_ge(main_done, tile_n(g, 0))
                    blocks(gi, first and gi < 2, range(EARLY))
                    if not (last and gi + 2 >= CB):
                        wait_product(sp, g, 3)
                        wait_product(sp, g, 5)
                        load_x(j, gi + 2)
                        load_right(j, gi + 2)
                    blocks(gi, False, range(EARLY, BQ))
                    if gi % 2 == 0 and not (last and gi + 4 >= CB):
                        sp.wait_ge(sq_ready, CP * j + gi // 2 + 1)
                        load_pair(j, gi // 2 + 2)
                    if gi == 2 and not first:
                        send(j - 1)
                    if first:
                        for p in pieces_of(gi):
                            if p + 1 < PIECES:
                                w1_load(p + 1)

            load_pair(0, 0)
            sp.dma_start(sel_raw, sel).then_inc(consts_in, 16)
            load_x(0, 0)
            sp.dma_start(w0a_raw, w0a).then_inc(consts_in, 16)
            sp.dma_start(w0b_raw, w0b).then_inc(consts_in, 16)
            load_right(0, 0)
            load_xd(0)
            sp.dma_start(idn[:, :], ident).then_inc(ident_in, 16)
            load_x(0, 1)
            load_pair(0, 1)
            sp.wait_ge(w0_ready, 3)
            load_right(0, 1)
            w1_load(0)
            chunk(0, True, False)
            with sp.Fori(1, NCH - 1) as j:
                chunk(j, False, False)
            chunk(NCH - 1, False, True)
            send(NCH - 1)
            sp.wait_ge(outs_dma, 16 * (NCH + 1))

        @block.tensor
        def _(pe):
            def fill_rep(j, gi, t, first):
                g = CB * j + gi
                if not (first and gi == 0):
                    wait_product(pe, g - 1, t)
                pn, u = CP * j + gi // 2, gi % 2
                if t == 0 and u == 0:
                    pe.wait_ge(x_low, pn + 1)
                nc.tensor.matmul(ring[:, SLOT[t], :], selr[:, u, REP.index(t), :], xhl[:, :],
                                 start=True, stop=True).then_inc(rep_done, 1)

            def fill_turn(g, gi, fresh):
                pe.wait_ge(x1_ready, g + 1)
                if not fresh:
                    pe.wait_ge(x1t_low, g)
                for q in range(NQ):
                    last = nc.tensor.transpose(ring[:, SLOT["turn"], q * H:(q + 1) * H],
                                               x1[:, q * P:(q + 1) * P], idn[:, :])
                last.then_inc(turned, 1)

            def main(j, gi, t, fresh):
                g = CB * j + gi
                if t == 0 and not fresh:
                    pe.wait_ge(x1_ready, g - 1)
                o = acc[:, gi % 2, :]
                if t in WHOLE:
                    wait_product(pe, g, t)
                    nc.tensor.matmul(o, w0w[:, WHOLE.index(t), :], fw[:, WHOLE.index(t), :], start=False, stop=False)\
                      .then_inc(main_done, 1)
                    return
                if t == FULL:
                    if gi % 2 == 0:
                        pe.wait_ge(sq_ready, CP * j + gi // 2 + 1)
                    nc.tensor.matmul(o, w0q[:, gi % 2, :], sq[:, :], start=False, stop=True).then_inc(main_done, 1)
                    return
                wait_high(pe, g, t)
                wait_low(pe, g, t)
                s = SPLIT.index(t)
                wh, wl = w0h[:, s, :], w0l[:, s, :]
                nc.tensor.matmul(o, wh, fh[:, s, :], start=t == 0, stop=False)
                nc.tensor.matmul(o, wl, fh[:, s, :], start=False, stop=False)
                nc.tensor.matmul(o, wh, fl[:, BUF[s], :], start=False, stop=False).then_inc(main_done, 1)

            def g_tile(j, g, gi, q, fresh, after_final):
                s = gi % 2
                if q == 0:
                    pe.wait_ge(x1t_low, g + 1)
                    pe.wait_ge(xbd_in[s], 16 * BQ * nth(j, gi, 2))
                    if after_final is not None:
                        pe.wait_ge(out2_ready, after_final)
                if not (fresh and q < 2):
                    pe.wait_ge(g_low, NQ * g + q - 1)
                o = pg[:, q % 2, 0:BQ * MI]
                xh = xbd[:, s, q, 0, :, :].rearrange("p b i -> p (b i)")
                xl = xbd[:, s, q, 1, :, :].rearrange("p b i -> p (b i)")
                nc.tensor.matmul(o, x1th[:, q, :], xh, start=True, stop=False)
                nc.tensor.matmul(o, x1th[:, q, :], xl, start=False, stop=False)
                nc.tensor.matmul(o, x1tl[:, q, :], xh, start=False, stop=True).then_inc(g_done, 1)

            def final(c):
                pe.wait_ge(g_low, CB * NQ * (c + 1))
                pe.wait_ge(w1_ready, PIECES)
                o = pg[:, 0, 0:NB]
                for i in range(M):
                    nc.tensor.matmul(o, w1h[:, i, :], gh[:, i, :], start=i == 0, stop=False)
                    nc.tensor.matmul(o, w1l[:, i, :], gh[:, i, :], start=False, stop=False)
                    last = nc.tensor.matmul(o, w1h[:, i, :], gl[:, i, :], start=False, stop=i == M - 1)
                last.then_inc(fin_done, 1)

            def chunk(j, first, last):
                for gi in range(CB):
                    g = CB * j + gi
                    for k in range(STEPS):
                        if k in FILL_AT:
                            for what in FILL_AT[k]:
                                if what == "turn":
                                    if not (first and gi == 0):
                                        fill_turn(g - 1, gi - 1, first and gi == 1)
                                elif not (last and gi == CB - 1):
                                    fill_rep(j if gi + 1 < CB else j + 1, (gi + 1) % CB, what, False)
                        if MAINS[k] is not None:
                            main(j, gi, MAINS[k], first and gi < 2)
                        if not (first and gi == 0):
                            for q in G_AT.get(k, ()):
                                g_tile(j, g - 1, gi - 1, q, first and gi == 1,
                                       j if gi == 1 and not first else None)
                        if k == FINAL_AT and gi == 1 and not first:
                            final(j - 1)

            pe.wait_ge(sel_ready, 1)
            fill_rep(0, 0, 0, True)
            fill_rep(0, 0, 2, True)
            fill_rep(0, 0, 4, True)
            pe.wait_ge(w0_ready, 3)
            pe.wait_ge(ident_in, 16)
            chunk(0, True, False)
            with pe.Fori(1, NCH - 1) as j:
                chunk(j, False, False)
            chunk(NCH - 1, False, True)
            fill_turn(NG - 1, CB - 1, False)
            for q in range(NQ):
                g_tile(NCH - 1, NG - 1, CB - 1, q, False, None)
            final(NCH - 1)

        @block.scalar
        def _(act):
            def high(g, gi, t, first):
                s = SPLIT.index(t)
                if not (first and gi == 0):
                    act.wait_ge(main_done, tile_n(g - 1, t))
                wait_product(act, g, t)
                nc.scalar.activation(fh[:, s, :], f[:, BUF[s], :], COPY).then_inc(high_done, 1)

            def squares(pn, pi, fresh):
                if not fresh:
                    act.wait_ge(main_done, tile_n(2 * pn - 1, FULL))
                nc.scalar.activation(sq[:, :], xp[:, pi % 2, :], SQUARE).then_inc(sq_high, 1)
                act.wait_ge(sq_high, 2 * pn + 1)
                act.wait_ge(x_low, pn + 1)
                nc.scalar.activation(xp[LO_ROW:P, pi % 2, :], xp[LO_ROW:P, pi % 2, :], SQUARE).then_inc(sq_high, 1)

            def x1_out(g, gi, fresh):
                act.wait_ge(main_done, tile_n(g, FULL))
                if not fresh:
                    act.wait_ge(turned, g)
                nc.scalar.activation(x1[:, :], acc[:, gi % 2, :], COPY).then_inc(x1_ready, 1)

            def x_split(j, pi, fresh):
                pn = CP * j + pi
                act.wait_ge(xp_in[pi % 2], 16 * (CP // 2 * j + pi // 2 + 1))
                if not fresh:
                    act.wait_ge(rep_done, len(REP) * 2 * pn)
                nc.scalar.activation(xhl[:, :], xp[:, pi % 2, :], COPY).then_inc(x_high, 1)

            def xd_split(j, gi, first):
                g = CB * j + gi
                act.wait_ge(xd_in, 16 * (g + 1))
                if not first:
                    act.wait_ge(xbd_in[gi % 2], 16 * BQ * (nth(j, gi, 2) - 1))
                nc.scalar.activation(xdhl[:, gi % 2, :, 0, :], xdr[:, :, :], COPY).then_inc(xd_high, 1)

            def turned_high(g, gi):
                act.wait_ge(turned, g + 1)
                nc.scalar.activation(x1th[:, :, :],
                                     ring[:, SLOT["turn"], :].rearrange("p (q h) -> p q h", h=H), COPY)\
                  .then_inc(x1t_high, 1)

            def g_high_part(g, gi, q, freed):
                act.wait_ge(g_done, NQ * g + q + 1)
                if q == 0 and freed is not None:
                    act.wait_ge(fin_done, freed)
                    act.wait_ge(out1_ready, freed)
                nc.scalar.activation(gh[:, :, g_at(gi, q)], g_psum(q), COPY).then_inc(g_high, 1)

            def final_out(c):
                act.wait_ge(fin_done, c + 1)
                act.wait_ge(outs_dma, 16 * (c + 1))
                nc.scalar.activation(outs[:, 1, :], pg[:, 0, 0:NB], COPY).then_inc(out2_ready, 1)

            def w1_piece(p):
                n = min(NW, M - NW * p)
                if p < PIECES - 1:
                    act.wait_ge(w1_in, 16 * (p + 1))
                else:
                    act.wait_ge(outs_dma, 16)
                nc.scalar.activation(w1h[:, NW * p:NW * p + n, :],
                                     outs[:, :, :].rearrange("p a b -> p (a b)")[:, 0:n * H], COPY)\
                  .then_inc(w1_high, 1)

            def chunk(j, first, last):
                for gi in range(CB):
                    g = CB * j + gi
                    prev = not (first and gi == 0)
                    more = not (last and gi == CB - 1)
                    pieces = pieces_of(gi) if first else ()
                    if prev:
                        x1_out(g - 1, gi - 1, first and gi == 1)
                    if prev and not (first and gi == 1):
                        g_high_part(g - 2, gi - 2, 3, None)
                    if prev:
                        turned_high(g - 1, gi - 1)
                    high(g, gi, 4, first)
                    high(g, gi, 5, first)
                    if gi % 2 == 0:
                        squares(CP * j + gi // 2, gi // 2, first and gi == 0)
                    for p in pieces[:1]:
                        w1_piece(p)
                    if gi == 1 and not first:
                        final_out(j - 1)
                    if prev:
                        g_high_part(g - 1, gi - 1, 0, j if gi == 1 and not first else None)
                        g_high_part(g - 1, gi - 1, 1, None)
                    if more:
                        high(g + 1, gi + 1, 0, False)
                    if gi % 2 == 0 and not (last and gi + 2 >= CB):
                        x_split(j, gi // 2 + 1, False)
                    if more:
                        high(g + 1, gi + 1, 2, False)
                    if more:
                        xd_split(j, gi + 1, first and gi == 0)
                    if prev:
                        g_high_part(g - 1, gi - 1, 2, None)
                    for p in pieces[1:]:
                        w1_piece(p)

            x_split(0, 0, True)
            act.wait_ge(consts_in, 48)
            nc.scalar.activation(selr[:, :, :, :], sel_raw.rearrange("p (u t m) -> p u t m", u=2, m=P), COPY)\
              .then_inc(sel_ready, 1)
            act.wait_ge(w0_sum, 1)
            n = len(SPLIT)
            nc.scalar.activation(w0h[:, :, :], w0a_raw[:, 0:n * H].rearrange("p (t h) -> p t h", h=H), COPY)\
              .then_inc(w0_high, 1)
            q_rows = slice(n * H, (n + 2) * H)
            nc.scalar.activation(x1th[:, 0:2, :], w0a_raw[:, q_rows].rearrange("p (t h) -> p t h", h=H), COPY)\
              .then_inc(w0_high, 1)
            nc.scalar.activation(w0q[:, :, :], w0b_raw[:, q_rows].rearrange("p (t h) -> p t h", h=H), COPY)\
              .then_inc(w0_high, 1)
            xd_split(0, 0, True)
            high(0, 0, 0, True)
            high(0, 0, 2, True)
            chunk(0, True, False)
            with act.Fori(1, NCH - 1) as j:
                chunk(j, False, False)
            chunk(NCH - 1, False, True)
            x1_out(NG - 1, CB - 1, False)
            g_high_part(NG - 2, CB - 2, 3, None)
            turned_high(NG - 1, CB - 1)
            for q in range(NQ):
                g_high_part(NG - 1, CB - 1, q, None)
            final_out(NCH - 1)

        @block.vector
        def _(dve):
            def product(j, gi, t, first):
                g = CB * j + gi
                if t == 0:
                    dve.wait_ge(xs_in[gi % XSB], 16 * nth(j, gi, XSB))
                if t in REP:
                    dve.wait_ge(rep_done, nth_of(REP, g, t))
                    right = ring[:, SLOT[t], :]
                else:
                    dve.wait_ge(xr_in[gi % 2], 16 * nth(j, gi, 2))
                    right = xr[:, gi % 2, LOADED.index(t), :]
                wait_f_free(dve, g, gi, t, first)
                nc.vector.tensor_tensor(f[:, BUF[SPLIT.index(t)], :], right, xs[:, gi % XSB, :], ALU.mult)\
                  .then_inc(prod_dve, 1)

            def low(g, gi, t, first):
                s = SPLIT.index(t)
                wait_high(dve, g, t)
                wait_fl_free(dve, g, gi, t, first)
                nc.vector.tensor_tensor(fl[:, BUF[s], :], f[:, BUF[s], :], fh[:, s, :], ALU.subtract)\
                  .then_inc(low_dve, 1)

            def squares_low(pn, pi):
                dve.wait_ge(sq_high, 2 * pn + 2)
                nc.vector.tensor_tensor(sq[LO_ROW:P, :], xp[LO_ROW:P, pi % 2, :], sq[LO_ROW:P, :], ALU.subtract)\
                  .then_inc(sq_ready, 1)

            def turned_low(g, gi):
                dve.wait_ge(x1t_high, g + 1)
                nc.vector.tensor_tensor(x1tl[:, :, :],
                                        ring[:, SLOT["turn"], :].rearrange("p (q h) -> p q h", h=H),
                                        x1th[:, :, :], ALU.subtract).then_inc(x1t_low, 1)

            def g_low_part(g, gi, q):
                dve.wait_ge(g_high, NQ * g + q + 1)
                nc.vector.tensor_tensor(gl[:, :, g_at(gi, q)], g_psum(q), gh[:, :, g_at(gi, q)],
                                        ALU.subtract).then_inc(g_low, 1)

            def chunk(j, first, last):
                for gi in range(CB):
                    g = CB * j + gi
                    prev = not (first and gi == 0)
                    more = not (last and gi == CB - 1)
                    product(j, gi, 4, first)
                    if prev and not (first and gi == 1):
                        g_low_part(g - 2, gi - 2, 3)
                    product(j, gi, 5, first)
                    if prev:
                        turned_low(g - 1, gi - 1)
                    low(g, gi, 4, first)
                    if more:
                        product(j, gi + 1, 0, False)
                        product(j, gi + 1, 2, False)
                    if prev:
                        g_low_part(g - 1, gi - 1, 0)
                        g_low_part(g - 1, gi - 1, 1)
                    if gi % 2 == 0:
                        squares_low(CP * j + gi // 2, gi // 2)
                    if more:
                        low(g + 1, gi + 1, 0, False)
                        low(g + 1, gi + 1, 2, False)
                    if prev:
                        g_low_part(g - 1, gi - 1, 2)

            dve.wait_ge(consts_in, 48)
            n = len(SPLIT)
            nc.vector.tensor_tensor(w0a_raw[:, 0:n * H], w0a_raw[:, 0:n * H], w0b_raw[:, 0:n * H],
                                    ALU.add).then_inc(w0_sum, 1)
            nc.vector.tensor_tensor(w0w[:, :, :],
                                    w0a_raw[:, (n + 2) * H:(n + 4) * H].rearrange("p (t h) -> p t h", h=H),
                                    w0b_raw[:, (n + 2) * H:(n + 4) * H].rearrange("p (t h) -> p t h", h=H),
                                    ALU.add).then_inc(w0_ready, 1)
            dve.wait_ge(w0_high, 3)
            nc.vector.tensor_tensor(w0l[:, :, :], w0a_raw[:, 0:n * H].rearrange("p (t h) -> p t h", h=H),
                                    w0h[:, :, :], ALU.subtract).then_inc(w0_ready, 1)
            last = w0b_raw[:, n * H:(n + 2) * H].rearrange("p (t h) -> p t h", h=H)
            nc.vector.tensor_tensor(last, last, w0q[:, :, :], ALU.subtract).then_inc(w0_sum, 1)
            dve.wait_ge(w0_sum, 2)
            nc.vector.tensor_tensor(w0q[:, :, :], last, x1th[:, 0:2, :], ALU.add).then_inc(w0_ready, 1)
            dve.wait_ge(w0_ready, 3)
            dve.wait_ge(sel_ready, 1)
            product(0, 0, 0, True)
            product(0, 0, 2, True)
            low(0, 0, 0, True)
            low(0, 0, 2, True)
            chunk(0, True, False)
            with dve.Fori(1, NCH - 1) as j:
                chunk(j, False, False)
            chunk(NCH - 1, False, True)
            g_low_part(NG - 2, CB - 2, 3)
            turned_low(NG - 1, CB - 1)
            for q in range(NQ):
                g_low_part(NG - 1, CB - 1, q)

        @block.gpsimd
        def _(pool):
            def product(j, gi, t, first):
                g = CB * j + gi
                pool.wait_ge(xr_in[gi % 2], 16 * nth(j, gi, 2))
                pool.wait_ge(xs_in[gi % XSB], 16 * nth(j, gi, XSB))
                wait_f_free(pool, g, gi, t, first)
                nc.gpsimd.tensor_tensor(fw[:, WHOLE.index(t), :], xr[:, gi % 2, LOADED.index(t), :], xs[:, gi % XSB, :],
                                        ALU.mult).then_inc(prod_pool, 1)

            def low(g, gi, t, first):
                s = SPLIT.index(t)
                wait_high(pool, g, t)
                wait_fl_free(pool, g, gi, t, first)
                nc.gpsimd.tensor_tensor(fl[:, BUF[s], :], f[:, BUF[s], :], fh[:, s, :], ALU.subtract)\
                  .then_inc(low_pool, 1)

            def x_split(pn, pi):
                pool.wait_ge(x_high, pn + 1)
                nc.gpsimd.tensor_tensor(xhl[LO_ROW:P, :], xp[LO_ROW:P, pi % 2, :],
                                        xhl[LO_ROW:P, :], ALU.subtract).then_inc(x_low, 1)

            def xd_split(g, gi):
                pool.wait_ge(xd_high, g + 1)
                nc.gpsimd.tensor_tensor(xdhl[:, gi % 2, :, 1, :], xdr[:, :, :], xdhl[:, gi % 2, :, 0, :],
                                        ALU.subtract).then_inc(xd_low, 1)

            def w1_piece(p):
                n = min(NW, M - NW * p)
                pool.wait_ge(w1_high, p + 1)
                nc.gpsimd.tensor_tensor(w1l[:, NW * p:NW * p + n, :],
                                        outs[:, :, :].rearrange("p a b -> p (a b)")[:, 0:n * H]
                                        .rearrange("p (n h) -> p n h", h=H),
                                        w1h[:, NW * p:NW * p + n, :], ALU.subtract).then_inc(w1_ready, 1)

            def first_out(c):
                pool.wait_ge(g_low, CB * NQ * (c + 1))
                pool.wait_ge(outs_dma, 16 * (c + 1))
                nc.gpsimd.tensor_tensor(outs[:, 0, :], gh[:, M, :], gl[:, M, :], ALU.add)\
                  .then_inc(out1_ready, 1)

            def chunk(j, first, last):
                for gi in range(CB):
                    g = CB * j + gi
                    more = not (last and gi == CB - 1)
                    pieces = pieces_of(gi) if first else ()
                    if gi == 1 and not first:
                        first_out(j - 1)
                    low(g, gi, 5, first)
                    for p in pieces[:1]:
                        w1_piece(p)
                    if more:
                        product(j, gi + 1, 1, False)
                    if gi % 2 == 0 and not (last and gi + 2 >= CB):
                        pn = CP * j + gi // 2 + 1
                        wait_product(pool, g + 1, 1)
                        x_split(pn, gi // 2 + 1)
                        pool.wait_ge(x_low, pn + 1)
                    if more:
                        product(j, gi + 1, 3, False)
                        xd_split(g + 1, gi + 1)
                    for p in pieces[1:]:
                        w1_piece(p)

            nc.gpsimd.memset(xbd[:, :, :, :, :, :].rearrange("p u q s b i -> p (u q s b i)").bitcast(F32), 0.0)\
              .then_inc(xbd_zero, 1)
            pool.wait_ge(xbd_zero, 1)
            x_split(0, 0)
            pool.wait_ge(x_low, 1)
            pool.wait_ge(w0_ready, 3)
            product(0, 0, 1, True)
            product(0, 0, 3, True)
            xd_split(0, 0)
            chunk(0, True, False)
            with pool.Fori(1, NCH - 1) as j:
                chunk(j, False, False)
            chunk(NCH - 1, False, True)
            first_out(NCH - 1)


def kernel(r_x, L0_rec_W0, L0_rec_W1):
    import concourse.bacc as bacc
    from concourse.bass_utils import run_bass_kernel_spmd

    x = np.asarray(r_x)
    w0 = np.asarray(L0_rec_W0).reshape(M, M, H)
    w1 = np.asarray(L0_rec_W1).reshape(M, H, H)
    xt = x.transpose(1, 0, 2).reshape(M, NG, GC)
    xa = np.ascontiguousarray(xt[np.arange(P) % M].transpose(1, 0, 2))
    rows = [*PICKED, *LEFT]
    xpairs = np.ascontiguousarray(np.tile(xt[rows].reshape(SUB, NG // 2, 2, GC).transpose(1, 2, 0, 3)
                                          .reshape(NG // 2, 2 * SUB, GC), (1, 2, 1)))
    xo = np.ones((B * D, MI), x.dtype)
    xo[:, 0:M] = x.transpose(0, 2, 1).reshape(B * D, M)
    xd = np.ascontiguousarray(xo.reshape(NG, NQ, P, MI).transpose(0, 2, 1, 3))
    right = np.zeros((FULL, P), np.int64)
    w0a = np.zeros((P, len(ORDER), H), w0.dtype)
    w0b = np.zeros((P, len(ORDER), H), w0.dtype)
    sel = np.zeros((P, 2, len(REP), P), np.float32)
    for t, m, i, j in pair_slots():
        w0a[m, ORDER.index(t)] = w0[i, j]
        if i != j:
            w0b[m, ORDER.index(t)] = w0[j, i]
        right[t, m] = j
        if t in REP:
            for u in range(2):
                for row in (0, LO_ROW):
                    sel[row + SUB * u + PICKED.index(j), u, REP.index(t), m] = 1.0
    for u in range(2):
        for m, i, what in left_rows(u):
            (w0b if what == "weight's low" else w0a)[m, ORDER.index(FULL) + u] = w0[i, i]
    xb = np.ascontiguousarray(xt[right[list(LOADED)]].transpose(2, 1, 0, 3))
    arrays = {
        "xa": xa, "xb": xb, "xd": xd, "xpairs": xpairs,
        "w0a": w0a.reshape(P, len(ORDER) * H), "w0b": w0b.reshape(P, len(ORDER) * H),
        "w1": np.ascontiguousarray(w1.transpose(1, 0, 2)).reshape(P, M * H),
        "sel": sel.reshape(P, 2 * len(REP) * P), "ident": np.eye(P, dtype=np.float32),
    }
    nc = bacc.Bacc("TRN2", target_bir_lowering=False, num_devices=1)
    args = [nc.dram_tensor(f"{n}_dram", a.shape, F32, kind="ExternalInput").ap() for n, a in arrays.items()]
    out = nc.dram_tensor("out_dram", (NCH, P, 2, NB), F32, kind="ExternalOutput").ap()
    build(nc, *args, out)
    r = run_bass_kernel_spmd(nc, [{f"{n}_dram": a for n, a in arrays.items()}], core_ids=[0])
    got = r.results[0]["out_dram"]
    return np.ascontiguousarray(got.transpose(0, 3, 2, 1)).reshape(B, 2 * H)
```
